# Optimizing a Trainium2 kernel written in Bass

```python
import numpy as np
import jax
import jax.numpy as jnp

def _softmax(x, axis=-1):
    return jax.nn.softmax(x, axis=axis)

def _gelu(x):
    return jax.nn.gelu(x, approximate=True)

def _silu(x):
    return jax.nn.silu(x)

def _sigmoid(x):
    return jax.nn.sigmoid(x)

def _layernorm(x, axis=-1, eps=1e-05):
    m = jnp.mean(x, axis=axis, keepdims=True)
    v = jnp.var(x, axis=axis, keepdims=True)
    return (x - m) / jnp.sqrt(v + eps)

def _scatter_add(tgt, idx, src, axis=0):
    return tgt.at[idx].add(src)

def _segment_sum(src, seg, n):
    return jax.ops.segment_sum(src, seg, n)
kernel_name = 'mk_cond_resid_d4_seqx_r4_3c4be1'

def setup_inputs(seed: int=0):
    np.random.seed(seed)
    _w = jnp.asarray

    def _rec_inputs():
        import jax
        import jax.numpy as jnp
        _rk = jax.random.key(seed)
        x = -0.0002071 + 1 * jax.random.normal(jax.random.fold_in(_rk, 1), (64, 64, 256), jnp.float32)
        _lenS = 64 - jax.random.randint(jax.random.fold_in(_rk, 7), (64,), 0, max(1, 64 // 4) + 1, jnp.int32)
        _lenS2 = 64 - jax.random.randint(jax.random.fold_in(_rk, 8), (64,), 0, max(1, 64 // 4) + 1, jnp.int32)
        cond_8 = jax.random.uniform(jax.random.fold_in(_rk, 11), (64, 8), jnp.float32, 0.0, 0.983423)
        return (x, cond_8)
    x, cond_8 = _rec_inputs()

    def _L0_cond_setup():
        import jax, jax.numpy as jnp
        import numpy as np
        R = 16
        ALPHA = 32.0
        SCALING = ALPHA / R
        key = jax.random.key(seed)
        ks = jax.random.split(key, 6)
        B, T, C, O, E = (16, 375, 256, 256, 8)
        x = jax.random.normal(ks[0], (B, T, C), dtype=jnp.float32)
        w = jax.random.uniform(ks[1], (B, E), dtype=jnp.float32)
        W_base = jax.random.normal(ks[2], (O, C), dtype=jnp.float32) * 0.02
        b_base = jax.random.normal(ks[3], (O,), dtype=jnp.float32) * 0.02
        As = jax.random.normal(ks[4], (E, R, C), dtype=jnp.float32) * 0.02
        Bs = jax.random.normal(ks[5], (E, O, R), dtype=jnp.float32) * 0.02
        return {'x': x, 'w': w, 'W_base': W_base, 'b_base': b_base, 'As': As, 'Bs': Bs}
    _L0_cond_all = _L0_cond_setup()
    _L0_cond_in = {k: v for k, v in _L0_cond_all.items() if k in ('W_base', 'b_base', 'As', 'Bs')}
    del _L0_cond_all

    def _L1_cond_setup():
        import jax, jax.numpy as jnp
        import numpy as np
        TOP_K = 2
        NUM_MOE_LAYERS = 12

        def _gemma_mlp(x, gate_w, up_w, down_w):
            g = jnp.einsum('bsh,hi->bsi', x, gate_w)
            u = jnp.einsum('bsh,hi->bsi', x, up_w)
            return jnp.einsum('bsi,ih->bsh', jax.nn.gelu(g, approximate=True) * u, down_w)
        key = jax.random.key(seed)
        ks = jax.random.split(key, 8)
        B, S, H, I, E = (32, 64, 256, 1024, 8)
        std = 0.02
        return {'x': jax.random.normal(ks[0], (B, S, H), jnp.float32), 'router_logits': jax.random.normal(ks[1], (B, E), jnp.float32), 'skill_gate': jax.random.normal(ks[2], (E, H, I), jnp.float32) * std, 'skill_up': jax.random.normal(ks[3], (E, H, I), jnp.float32) * std, 'skill_down': jax.random.normal(ks[4], (E, I, H), jnp.float32) * std, 'shared_gate': jax.random.normal(ks[5], (H, I), jnp.float32) * std, 'shared_up': jax.random.normal(ks[6], (H, I), jnp.float32) * std, 'shared_down': jax.random.normal(ks[7], (I, H), jnp.float32) * std}
    _L1_cond_all = _L1_cond_setup()
    _L1_cond_in = {k: v for k, v in _L1_cond_all.items() if k in ('skill_gate', 'skill_up', 'skill_down', 'shared_gate', 'shared_up', 'shared_down')}
    del _L1_cond_all

    def _L2_cond_setup():
        import jax, jax.numpy as jnp
        import numpy as np
        key = jax.random.key(seed)
        k1, k2, k3, k4, k5 = jax.random.split(key, 5)
        B, N, T, O, G = (32, 64, 256, 256, 8)
        x = jax.random.normal(k1, (B, N, T), dtype=jnp.float32)
        y = jax.random.uniform(k2, (B, G), dtype=jnp.float32)
        weight = jax.random.normal(k3, (G, O, T), dtype=jnp.float32) * (1.0 / np.sqrt(T))
        mask = jax.random.uniform(k4, (O, T), dtype=jnp.float32)
        bias = jax.random.normal(k5, (O,), dtype=jnp.float32)
        return {'x': x, 'y': y, 'weight': weight, 'mask': mask, 'bias': bias}
    _L2_cond_all = _L2_cond_setup()
    _L2_cond_in = {k: v for k, v in _L2_cond_all.items() if k in ('weight', 'mask', 'bias')}
    del _L2_cond_all

    def _L3_cond_setup():
        import jax, jax.numpy as jnp
        import numpy as np
        B, S, D = (16, 512, 256)
        E, H = (8, 512)
        key = jax.random.key(seed)
        ks = jax.random.split(key, 8)
        scale = 0.02
        x = jax.random.normal(ks[0], (B, S, D), dtype=jnp.float32)
        opcode_onehot = jax.random.uniform(ks[1], (B, E), dtype=jnp.float32)
        W_up = jax.random.normal(ks[2], (E, H, D), dtype=jnp.float32) * scale
        b_up = jnp.zeros((E, H), dtype=jnp.float32)
        W_gate = jax.random.normal(ks[3], (E, H, D), dtype=jnp.float32) * scale
        b_gate = jnp.zeros((E, H), dtype=jnp.float32)
        W_down = jax.random.normal(ks[4], (E, D, H), dtype=jnp.float32) * scale
        b_down = jnp.zeros((E, D), dtype=jnp.float32)
        return {'x': x, 'opcode_onehot': opcode_onehot, 'W_up': W_up, 'b_up': b_up, 'W_gate': W_gate, 'b_gate': b_gate, 'W_down': W_down, 'b_down': b_down}
    _L3_cond_all = _L3_cond_setup()
    _L3_cond_in = {k: v for k, v in _L3_cond_all.items() if k in ('W_up', 'b_up', 'W_gate', 'b_gate', 'W_down', 'b_down')}
    del _L3_cond_all
    return {'x': x, 'cond_8': cond_8, 'L0_cond_W_base': _L0_cond_in['W_base'], 'L0_cond_b_base': _L0_cond_in['b_base'], 'L0_cond_As': _L0_cond_in['As'], 'L0_cond_Bs': _L0_cond_in['Bs'], 'L1_cond_skill_gate': _L1_cond_in['skill_gate'], 'L1_cond_skill_up': _L1_cond_in['skill_up'], 'L1_cond_skill_down': _L1_cond_in['skill_down'], 'L1_cond_shared_gate': _L1_cond_in['shared_gate'], 'L1_cond_shared_up': _L1_cond_in['shared_up'], 'L1_cond_shared_down': _L1_cond_in['shared_down'], 'L2_cond_weight': _L2_cond_in['weight'], 'L2_cond_mask': _L2_cond_in['mask'], 'L2_cond_bias': _L2_cond_in['bias'], 'L3_cond_W_up': _L3_cond_in['W_up'], 'L3_cond_b_up': _L3_cond_in['b_up'], 'L3_cond_W_gate': _L3_cond_in['W_gate'], 'L3_cond_b_gate': _L3_cond_in['b_gate'], 'L3_cond_W_down': _L3_cond_in['W_down'], 'L3_cond_b_down': _L3_cond_in['b_down']}

def reference(x, cond_8, L0_cond_W_base, L0_cond_b_base, L0_cond_As, L0_cond_Bs, L1_cond_skill_gate, L1_cond_skill_up, L1_cond_skill_down, L1_cond_shared_gate, L1_cond_shared_up, L1_cond_shared_down, L2_cond_weight, L2_cond_mask, L2_cond_bias, L3_cond_W_up, L3_cond_b_up, L3_cond_W_gate, L3_cond_b_gate, L3_cond_W_down, L3_cond_b_down):
    import jax
    import jax.numpy as jnp

    def _L0_cond_ref(x, w, W_base, b_base, As, Bs):
        import jax, jax.numpy as jnp
        import numpy as np
        R = 16
        ALPHA = 32.0
        SCALING = ALPHA / R
        out = jnp.einsum('btc,oc->bto', x, W_base) + b_base
        h = jnp.einsum('btc,erc->bter', x, As)
        lora = jnp.einsum('bter,eor,be->bto', h, Bs, w)
        return out + lora * SCALING

    def _L1_cond_ref(x, router_logits, skill_gate, skill_up, skill_down, shared_gate, shared_up, shared_down):
        import jax, jax.numpy as jnp
        import numpy as np
        TOP_K = 2
        NUM_MOE_LAYERS = 12

        def _gemma_mlp(x, gate_w, up_w, down_w):
            g = jnp.einsum('bsh,hi->bsi', x, gate_w)
            u = jnp.einsum('bsh,hi->bsi', x, up_w)
            return jnp.einsum('bsi,ih->bsh', jax.nn.gelu(g, approximate=True) * u, down_w)
        B = x.shape[0]
        E = skill_gate.shape[0]
        rw = jax.nn.softmax(router_logits.astype(jnp.float32), axis=-1)
        w, sel = jax.lax.top_k(rw, TOP_K)
        w = w / w.sum(axis=-1, keepdims=True)
        w = w.astype(x.dtype)
        scale = 1.0 / NUM_MOE_LAYERS
        w = scale * w + (1.0 - scale) * jax.lax.stop_gradient(w)
        dense_w = jnp.zeros((B, E), x.dtype).at[jnp.arange(B)[:, None], sel].add(w)

        def step(acc, params):
            g, u, d, we = params
            return (acc + we[:, None, None] * _gemma_mlp(x, g, u, d), None)
        out, _ = jax.lax.scan(step, jnp.zeros_like(x), (skill_gate, skill_up, skill_down, dense_w.T))
        out = out + _gemma_mlp(x, shared_gate, shared_up, shared_down)
        return out

    def _L2_cond_ref(x, y, weight, mask, bias):
        import jax, jax.numpy as jnp
        import numpy as np
        masked_w = weight * mask[None, :, :]
        w_bot = jnp.einsum('bg,got->bot', y, masked_w)
        return jnp.einsum('bnt,bot->bno', x, w_bot) + bias

    def _L3_cond_ref(x, opcode_onehot, W_up, b_up, W_gate, b_gate, W_down, b_down):
        import jax, jax.numpy as jnp
        import numpy as np
        B, S, D = (16, 512, 256)
        E, H = (8, 512)
        expert = jnp.argmax(opcode_onehot, axis=-1)
        wu, bu = (W_up[expert], b_up[expert])
        wg, bg = (W_gate[expert], b_gate[expert])
        wd, bd = (W_down[expert], b_down[expert])
        up = jnp.einsum('bsd,bhd->bsh', x, wu) + bu[:, None, :]
        gate = jnp.einsum('bsd,bhd->bsh', x, wg) + bg[:, None, :]
        hidden = jax.nn.silu(up) * gate
        out = jnp.einsum('bsh,bdh->bsd', hidden, wd) + bd[:, None, :]
        return out
    x = x + _L0_cond_ref(x, cond_8, L0_cond_W_base, L0_cond_b_base, L0_cond_As, L0_cond_Bs)
    x = x + _L1_cond_ref(x, cond_8, L1_cond_skill_gate, L1_cond_skill_up, L1_cond_skill_down, L1_cond_shared_gate, L1_cond_shared_up, L1_cond_shared_down)
    x = x + _L2_cond_ref(x, cond_8, L2_cond_weight, L2_cond_mask, L2_cond_bias)
    x = x + _L3_cond_ref(x, cond_8, L3_cond_W_up, L3_cond_b_up, L3_cond_W_gate, L3_cond_b_gate, L3_cond_W_down, L3_cond_b_down)
    return x

_drawn_inputs = setup_inputs


def setup_inputs(seed=0):
    import zlib

    import numpy as np

    out = dict(_drawn_inputs(seed))
    spreads = {'L3_cond_b_up': (0.0, 0.8), 'L3_cond_b_gate': (0.0, 0.8), 'L3_cond_b_down': (0.0, 0.1)}
    factors = {'L0_cond_b_base': 4.194, 'L1_cond_skill_gate': 2.715}
    for name, (base, spread) in spreads.items():
        noise = np.random.default_rng([zlib.crc32(name.encode()), seed]).standard_normal(out[name].shape)
        drawn = base * np.exp(spread * noise) if base else spread * noise
        out[name] = jnp.asarray(drawn.astype(out[name].dtype))
    for name, factor in factors.items():
        out[name] = (out[name] * factor).astype(out[name].dtype)
    return out
```

```python
from contextlib import ExitStack

import concourse.bass as bass
from concourse import mybir

F32 = mybir.dt.float32
F16 = mybir.dt.float16
I32 = mybir.dt.int32
U32 = mybir.dt.uint32
ALU = mybir.AluOpType
ACT = mybir.ActivationFunctionType
AX = mybir.AxisListType.X
ds = bass.ds

P = 128
B = 64
T = 64
K = 2
D = K * P
E = 8
R = P // E
I1 = 1024
IC1 = I1 // P
H3 = 512
HC3 = H3 // P
GB = 4
GN = GB * T
TB = 8
TN = TB * T
NT = B // TB
SH = B // GB
G1 = 2 * B // GB + E + SH
S1 = G1 * GB
G3 = B // GB + E
S3 = G3 * GB
XSC = 16.0
WSC = 256.0
INV = 1.0 / (XSC * WSC)
NQ = 4
QB = B // NQ
OG = D // R
NSTAGE = 3
PIECE = 1024
TOP_SCALE = 1.0 / 12.0
GB_LOG = 2
N1P = 6
N2_0 = 1 + (E + 1) * N1P
N2P = 4
N3_0 = N2_0 + N2P
N3P = 3
CONSTS = 19
TABLES = 3
SMALL = E + 5


def build(nc, a, out):
    with ExitStack() as ctx:
        def sb(name, shape, dt):
            return ctx.enter_context(nc.sbuf_tensor(name, shape, dt))

        def ps(name, shape):
            return ctx.enter_context(nc.psum_tensor(name, shape, F32))

        def sem(name):
            return ctx.enter_context(nc.semaphore(name))

        XR = sb("XR", [P, B + 1, K, T], F32)
        XS = sb("XS", [P, B + 1, 2, K, T], F16)
        U = sb("U", [P, 2 * 2 * K * QB * D], F16)
        W3 = sb("W3", [P, 2, 3, 2, HC3 * D], F16)
        XG = sb("XG", [P, 2 * GB * 2 * K * T], F16)
        GL = sb("GL", [P, 2, 2 * GN], F32)
        HF = sb("HF", [P, 2, 2 * GN], F32)
        HS = sb("HS", [P, 2, IC1 * GN], F16)
        ST = sb("ST", [P, NSTAGE, PIECE], F32)
        WM = sb("WM", [P, 2, OG * D], F16)
        YB = sb("YB", [P, 2, B * R], F16)
        WF = sb("WF", [P, 1], F32)
        BI = sb("BI", [P, 2 * K], F32)
        BU = sb("BU", [P, E, HC3], F32)
        BG = sb("BG", [P, E, HC3], F32)
        BD = sb("BD", [P, E, K], F32)
        WS = sb("WS", [P, S1], F32)
        SL1 = sb("SL1", [1, S1], I32)
        SL3 = sb("SL3", [1, S3], I32)
        ST1 = sb("ST1", [1, E + 2], I32)
        ST3 = sb("ST3", [1, E + 1], I32)
        UW1 = 2 * 2 * 3 * K * I1
        W0 = U[:, UW1:UW1 + 2 * PIECE].rearrange("p (h n) -> p h n", h=2)
        MK = U[:, UW1 + 2 * PIECE:UW1 + 4 * PIECE].bitcast(F32)
        small = U[:, UW1 + 4 * PIECE:].bitcast(F32)
        YR = small[:, 0:B]
        CW = small[:, B:2 * B]
        DG = small[:, 2 * B:2 * B + R]
        scratch = small[0:B, 2 * B + R:]
        OV = U[:, 0:2 * K * GN].bitcast(F32).rearrange("p (o n) -> p o n", o=K)
        at = [0]

        def rt(n):
            at[0] += n
            assert at[0] <= scratch.shape[1]
            return scratch[:, at[0] - n:at[0]]

        IO = rt(S1)
        TRI = rt(B)
        ONE = rt(P)
        BM = rt(P)
        LG = rt(E)
        SO = rt(8)
        MI = rt(8)
        MIF = rt(8)
        EX = rt(8)
        DD = rt(8)
        SM = rt(8)
        M1 = rt(E)
        M2 = rt(E)
        MM = rt(E + 1)
        WD = rt(E + 1)
        RK = rt(E + 1)
        CN = rt(E + 1)
        CI = rt(E + 1)
        SF = rt(E + 2)
        PO_ = rt(E + 1)
        EQ = rt(2 * S1)
        EQW = rt(2 * S1)
        YF = HF[:, :, :].rearrange("p a n -> p (a n)")
        assert B * R == 2 * 2 * GN

        pG = ps("pG", [P, 2, 512])
        pU = ps("pU", [P, 2, 512])
        pO = ps("pO", [P, 2, 512])
        pA = ps("pA", [P, 2, 512])

        def w1(par, which, hl):
            n = K * I1
            o = ((par * 3 + which) * 2 + hl) * n
            return U[:, o:o + n]

        WB = U[:, :].rearrange("p (r h k b o) -> p r h k b o", r=2, h=2, k=K, b=QB)
        XGv = XG[:, :].rearrange("p (r s h k t) -> p r s h k t", r=2, s=GB, h=2, k=K)
        XGd = XG[:, :].rearrange("p (r s n) -> p r s n", r=2, s=GB)
        XSd = XS[:, :, :, :, :].rearrange("p b h k t -> p b (h k t)")
        XRd = XR[:, :, :, :].rearrange("p b k t -> p b (k t)")
        HSv = HS[:, :, :].rearrange("p h (c n) -> p h c n", c=IC1)

        x_in = [sem(f"x_in{i}") for i in range(NT)]
        cond_in = sem("cond_in")
        small_in = sem("small_in")
        st_in = [sem(f"st_in{i}") for i in range(NSTAGE)]
        mk_in = sem("mk_in")
        masked = sem("masked")
        scaled = sem("scaled")
        w_ready = sem("w_ready")
        consts = sem("consts")
        tables = sem("tables")
        dve_step = sem("dve_step")
        r_exp = sem("r_exp")
        r_ex = sem("r_ex")
        r_eq = sem("r_eq")
        r_eqd = sem("r_eqd")
        r_mm = sem("r_mm")
        r_out = sem("r_out")
        xs_hi = sem("xs_hi")
        xs_ready = sem("xs_ready")
        h0_mm = sem("h0_mm")
        h0_f = sem("h0_f")
        h0_hi = sem("h0_hi")
        h0_ready = sem("h0_ready")
        o0_mm = sem("o0_mm")
        o0_free = sem("o0_free")
        o0_add = sem("o0_add")
        b_mm = sem("b_mm")
        b_hi = sem("b_hi")
        b_ready = sem("b_ready")
        o2_mm = sem("o2_mm")
        o2_ev = sem("o2_ev")
        o2_add = sem("o2_add")
        y_out = sem("y_out")

        def group_sems(n):
            names = ("xg_in", "xg_free", "gate_mm", "up_mm", "act_done", "gu_free", "h_hi", "h_ready",
                     "h_free", "o_free", "added")
            return {x: sem(f"{x}{n}") for x in names}

        L1s, L3s = group_sems(1), group_sems(3)

        def group_loop(eng, starts, e):
            most = G1 if starts is ST1 else G3
            first = eng.value_load(starts[0:1, ds(e, 1)], min_val=0, max_val=most - 1)
            end = eng.value_load(starts[0:1, ds(e + 1, 1)], min_val=1, max_val=most)
            return eng.Fori(first, end, 1)

        def wait_alone(eng, s, value):
            eng.wait_ge(s, value)
            eng.nop(nofuse=True)

        block = ctx.enter_context(nc.Block())

        @block.sync
        def _(sp):
            sp.dma_start(LG, a["cond_8"]).then_inc(cond_in, 16)
            for t in range(NT):
                tile = slice(t * TB, (t + 1) * TB)
                sp.dma_start(XRd[:, tile, :], a["x"][:, tile, :]).then_inc(x_in[t], 16)

            def gathers(starts, slots, e, q):
                with group_loop(sp, starts, e) as i:
                    sp.wait_ge(q["xg_free"], i + 1)
                    par = sp.snap(i & 1)
                    for s in range(GB):
                        b = sp.value_load(slots[0:1, ds(i * GB + s, 1)], min_val=0, max_val=B)
                        sp.dma_start(XGd[:, ds(par, 1), s, :], XSd[:, ds(b, 1), :]).then_inc(q["xg_in"], 16)
                    wait_alone(sp, q["xg_in"], (i + 1) * (16 * GB))

            sp.wait_ge(r_out, 2)
            sp.wait_ge(consts, CONSTS)
            sp.wait_ge(xs_ready, 2 * NT)
            with sp.Fori(0, E + 1, 1) as e:
                gathers(ST1, SL1, e, L1s)
            sp.wait_ge(xs_ready, 4 * NT)
            with sp.Fori(0, E, 1) as e:
                gathers(ST3, SL3, e, L3s)
            n3 = sp.value_load(ST3[0:1, E:E + 1], min_val=1, max_val=G3)
            sp.wait_ge(L3s["added"], n3 * GB + 1)
            sp.dma_start(out, XRd[:, 0:B, :]).then_inc(y_out, 16)
            sp.wait_ge(y_out, 16)

        @block.gpsimd
        def _(pool):
            def load(n, j, src):
                view = ST[:, j, :]
                if len(src.shape) == 3:
                    view = view.rearrange("p (c n) -> p c n", c=src.shape[1])
                pool.dma_start(view, src).then_inc(st_in[j], 16)

            def convert(n, turn, j, hi, lo, mask=None):
                src = ST[:, j, :]
                wait_alone(pool, st_in[j], turn * 16 + 16)
                if mask is not None:
                    pool.wait_ge(mk_in, 16 * E * (mask + 1))
                    nc.gpsimd.tensor_tensor(src, src, MK[:, :], ALU.mult).then_inc(masked, 1)
                    pool.wait_ge(masked, mask + 1)
                factor = WF[:, :].to_broadcast([P, PIECE])
                nc.gpsimd.tensor_tensor(hi, src, factor, ALU.mult)
                nc.gpsimd.tensor_tensor(src, src, factor, ALU.mult).then_inc(scaled, 1)
                pool.wait_ge(scaled, n + 1)
                nc.gpsimd.tensor_tensor(lo, src, hi, ALU.subtract).then_inc(w_ready, 1)

            def run(n0, jt, srcs, dsts, masks=None):
                if not isinstance(n0, int) or n0:
                    wait_alone(pool, w_ready, n0)
                for m in range(min(NSTAGE, len(srcs))):
                    load(n0 + m, jt(m)[0], srcs[m])
                for m in range(len(srcs)):
                    j, turn = jt(m)
                    if masks is not None:
                        if m:
                            pool.wait_ge(masked, m)
                        for g in range(E):
                            pool.dma_start(MK[g * R:(g + 1) * R, :], masks[m]).then_inc(mk_in, 16)
                    convert(n0 + m, turn, j, *dsts[m], mask=None if masks is None else m)
                    if m + NSTAGE < len(srcs):
                        wait_alone(pool, w_ready, n0 + m + 1)
                        load(n0 + m + NSTAGE, j, srcs[m + NSTAGE])

            def static(n0):
                return lambda m: ((n0 + m) % NSTAGE, (n0 + m) // NSTAGE)

            for g in range(E):
                pool.dma_start(YR[g * R:(g + 1) * R, :],
                               a["condT"][g:g + 1, :].partition_broadcast(R)).then_inc(small_in, 16)
            for t, src in ((BI[:, 0:K], a["L0_cond_b_base"]), (BI[:, K:], a["L2_cond_bias"]),
                           (BU[:, :, :], a["L3_cond_b_up"]), (BG[:, :, :], a["L3_cond_b_gate"]),
                           (BD[:, :, :], a["L3_cond_b_down"])):
                pool.dma_start(t, src).then_inc(small_in, 16)

            nc.gpsimd.iota(IO.bitcast(I32), [[1, S1]], 0, 0).then_inc(consts, 1)
            nc.gpsimd.iota(BM.bitcast(I32), [[0, P]], -B, 1).then_inc(consts, 1)
            nc.gpsimd.memset(WF[:, :], WSC).then_inc(consts, 1)
            nc.gpsimd.memset(ONE, 1.0).then_inc(consts, 1)
            nc.gpsimd.memset(TRI, 1.0).then_inc(consts, 1)
            nc.gpsimd.memset(DG[:, :], 0.0).then_inc(consts, 1)
            pool.wait_ge(consts, 6)
            nc.gpsimd.tensor_copy(IO, IO.bitcast(I32)).then_inc(consts, 1)
            nc.gpsimd.tensor_copy(BM, BM.bitcast(I32)).then_inc(consts, 1)
            nc.gpsimd.affine_select(out=TRI, in_=TRI, compare_op=ALU.is_gt, fill=0.0, base=0,
                                    pattern=[[1, B]], channel_multiplier=-1).then_inc(consts, 1)
            for g in range(E):
                pool.wait_ge(consts, 9 + g)
                nc.gpsimd.affine_select(out=DG[:, :], in_=DG[:, :], compare_op=ALU.not_equal, fill=1.0,
                                        base=-R * g, pattern=[[-1, R]], channel_multiplier=1).then_inc(consts, 1)
            nc.gpsimd.memset(XR[:, B, :, :], 0.0).then_inc(consts, 1)
            nc.gpsimd.memset(XS[:, B, :, :, :], 0.0).then_inc(consts, 1)

            run(0, static(0), [a["w0"]], [(W0[:, 0, :], W0[:, 1, :])])

            def w1_dsts(par):
                return [(w1(par, m // 2, 0)[:, (m % 2) * PIECE:(m % 2 + 1) * PIECE],
                         w1(par, m // 2, 1)[:, (m % 2) * PIECE:(m % 2 + 1) * PIECE]) for m in range(N1P)]

            def w1_srcs(g, u, d):
                half = d.rearrange("(c p) h -> p c h", p=P)
                return [g[0:P, :], g[P:, :], u[0:P, :], u[P:, :],
                        half[:, 0:IC1 // 2, :], half[:, IC1 // 2:, :]]

            def w1_jt(e):
                return lambda m: ((1 + m) % NSTAGE, e * (N1P // NSTAGE) + (1 + m) // NSTAGE)

            def expert1(e, par):
                run(e * N1P + 1, w1_jt(e), w1_srcs(*(a[n][ds(e, 1)].rearrange("e k n -> (e k) n") for n in
                    ("L1_cond_skill_gate", "L1_cond_skill_up", "L1_cond_skill_down"))), w1_dsts(par))

            def buffer_free(starts, e, q):
                done = pool.value_load(starts[0:1, ds(e - 1, 1)], min_val=1, max_val=G1)
                wait_alone(pool, q["h_free"], (done + 1) * (IC1 // 2 if starts is ST1 else HC3 // 2))

            for e in (0, 1):
                expert1(e, e)
            pool.wait_ge(r_out, 2)
            with pool.Fori(1, E // 2, 1) as ep:
                for par in (0, 1):
                    buffer_free(ST1, ep * 2 + par, L1s)
                    expert1(ep * 2 + par, par)
            buffer_free(ST1, E, L1s)
            run(E * N1P + 1, w1_jt(E), w1_srcs(a["L1_cond_shared_gate"], a["L1_cond_shared_up"],
                                               a["L1_cond_shared_down"]), w1_dsts(0))

            run(N2_0, static(N2_0), [a["w2"][:, m * PIECE:(m + 1) * PIECE] for m in range(N2P)],
                [(WM[:, 0, m * PIECE:(m + 1) * PIECE], WM[:, 1, m * PIECE:(m + 1) * PIECE]) for m in range(N2P)],
                [a["mask"][:, m * PIECE:(m + 1) * PIECE] for m in range(N2P)])

            def expert3(e, par):
                run(e * N3P + N3_0, lambda m: ((N3_0 + m) % NSTAGE, e + (N3_0 + m) // NSTAGE),
                    [a[n][ds(e, 1)].rearrange("e p n -> (e p) n") for n in
                     ("L3_cond_W_up", "L3_cond_W_gate", "L3_cond_W_down")],
                    [(W3[:, par, m, 0, :], W3[:, par, m, 1, :]) for m in range(N3P)])

            for e in (0, 1):
                expert3(e, e)
            with pool.Fori(1, E // 2, 1) as ep:
                for par in (0, 1):
                    buffer_free(ST3, ep * 2 + par, L3s)
                    expert3(ep * 2 + par, par)

        @block.tensor
        def _(pe):
            def three(o, whi, wlo, xhi, xlo, first, last):
                nc.tensor.matmul(o, whi, xhi, start=first, stop=False)
                nc.tensor.matmul(o, whi, xlo, start=False, stop=False)
                return nc.tensor.matmul(o, wlo, xhi, start=False, stop=last)

            pe.wait_ge(consts, CONSTS)
            for layer, (ne, ns) in enumerate(((E + 1, S1), (E, S3))):
                pe.wait_ge(r_exp, 2 * layer + 2)
                nc.tensor.matmul(pA[0:B, 0, 0:ne], TRI, MM[:, 0:ne], start=True, stop=True)
                nc.tensor.matmul(pA[0:B, 1, 0:ne], ONE[:, 0:B], MM[:, 0:ne], start=True, stop=True).then_inc(r_mm, 1)
                for e in range(ne):
                    pe.wait_ge(r_eq, layer * (E + 1) + e + 1)
                    q = e % 2
                    nc.tensor.matmul(pO[:, 0, 0:ns], BM, EQ[:, q * S1:q * S1 + ns], start=(e == 0), stop=(e == ne - 1))
                    nc.tensor.matmul(pO[:, 1, 0:ns], ONE, EQW[:, q * S1:q * S1 + ns], start=(e == 0),
                                     stop=(e == ne - 1)).then_inc(r_eqd, 1)

            pe.wait_ge(w_ready, 1)
            pe.wait_ge(r_out, 2)
            wb = [W0[:, q, 0:K * D].rearrange("p (k o) -> p k o", k=K) for q in range(2)]
            wa = [W0[:, q, K * D:K * D + K * P].rearrange("p (k m) -> p k m", k=K) for q in range(2)]
            wc = [W0[:, q, K * D + K * P:] for q in range(2)]
            h0 = [HS[:, q, 0:TN] for q in range(2)]

            def tile0(t, par):
                xs = XS[:, ds(t * TB, TB), :, :, :]
                pe.wait_ge(xs_ready, t + 1)
                for k in range(K):
                    mm = three(pA[:, par, :], wa[0][:, k, :], wa[1][:, k, :], xs[:, :, 0, k, :], xs[:, :, 1, k, :],
                               k == 0, k == K - 1)
                mm.then_inc(h0_mm, 1)
                pe.wait_ge(o0_free, t + 1)
                for o in range(K):
                    for k in range(K):
                        three(pO[:, o, :], wb[0][:, k, o * P:(o + 1) * P], wb[1][:, k, o * P:(o + 1) * P],
                              xs[:, :, 0, k, :], xs[:, :, 1, k, :], k == 0, False)
                pe.wait_ge(h0_ready, t + 1)
                for o in range(K):
                    mm = three(pO[:, o, :], wc[0][:, o * P:(o + 1) * P], wc[1][:, o * P:(o + 1) * P],
                               h0[0], h0[1], False, True)
                mm.then_inc(o0_mm, 1)

            with pe.Fori(0, NT // 2, 1) as tp:
                for par in (0, 1):
                    tile0(pe.snap(tp * 2 + par), par)

            def gate_up(q, i, p, x, gate, up, kc):
                pe.wait_ge(q["gu_free"], i * kc + p + 1)
                products = ((pG, gate, q["gate_mm"]), (pU, up, q["up_mm"]))
                for dst, w, done in products if q is L1s else products[::-1]:
                    for c in (0, 1):
                        for k in range(K):
                            mm = three(dst[:, p % 2, c * GN:(c + 1) * GN], w(0, k, 2 * p + c), w(1, k, 2 * p + c),
                                       x[0][k], x[1][k], k == 0, k == K - 1)
                    mm.then_inc(done, 1)

            def down(q, i, p, w, kc):
                pe.wait_ge(q["h_ready"], i * kc + p + 1)
                if p == 0 and q is L1s:
                    pe.wait_ge(q["added"], i * GB + 1)
                elif p == 0:
                    pe.wait_ge(q["o_free"], i + 1)
                for c in (0, 1):
                    h = 2 * p + c
                    for o in range(K):
                        mm = three(pO[:, o, 0:GN], w(0, h, o), w(1, h, o), HSv[:, 0, h, :], HSv[:, 1, h, :],
                                   h == 0, h == 2 * kc - 1)
                        if p == kc - 2 and c == o == 0:
                            mm.then_inc(q["xg_free"], 1)
                mm.then_inc(q["h_free"], 1)

            def groups(q, starts, e, gate, up, dn, kc, order):
                with group_loop(pe, starts, e) as i:
                    pe.wait_ge(q["xg_in"], (i + 1) * (16 * GB))
                    par = pe.snap(i & 1)
                    x = [[XGv[:, ds(par, 1), :, h, k, :] for k in range(K)] for h in range(2)]
                    for kind, p in order:
                        if kind == "gu":
                            gate_up(q, i, p, x, gate, up, kc)
                        else:
                            down(q, i, p, dn, kc)

            ORDER1 = [("gu", 0), ("gu", 1), ("d", 0), ("gu", 2), ("gu", 3), ("d", 1), ("d", 2), ("d", 3)]
            ORDER3 = [("gu", 0), ("gu", 1), ("d", 0), ("d", 1)]

            def expert1(e, par):
                wait_alone(pe, w_ready, e * N1P + N1P + 1)
                gu = [lambda h, k, c, m=m: w1(par, m, h)[:, k * I1 + c * P:k * I1 + (c + 1) * P] for m in (0, 1)]
                dn = lambda h, c, o: w1(par, 2, h)[:, c * D + o * P:c * D + (o + 1) * P]
                groups(L1s, ST1, e, gu[0], gu[1], dn, IC1 // 2, ORDER1)

            pe.wait_ge(o0_free, NT + 1)
            with pe.Fori(0, E // 2, 1) as ep:
                for par in (0, 1):
                    expert1(pe.snap(ep * 2 + par), par)
            expert1(E, 0)

            pe.wait_ge(w_ready, N2_0 + N2P)
            pe.wait_ge(tables, TABLES)
            def mix(qt, og):
                n = qt * OG + og
                bank = (pG, pU)[n // 2 % 2][:, n % 2, :]
                if n >= 4:
                    pe.wait_ge(b_ready, n - 3)
                ys = [YB[:, h, qt * QB * R:(qt + 1) * QB * R] for h in range(2)]
                for k in range(K):
                    wm = [WM[:, h, og * D + k * P:og * D + (k + 1) * P] for h in range(2)]
                    mm = three(bank[:, k * QB * R:(k + 1) * QB * R], wm[0], wm[1], ys[0], ys[1], True, True)
                mm.then_inc(b_mm, 1)

            def apply(qt, j):
                bb = qt * QB + j
                n, b = bb // TB, bb % TB
                if j == 0:
                    pe.wait_ge(b_ready, (qt + 1) * OG)
                if b == 0 and n >= 2:
                    pe.wait_ge(o2_ev, n - 1)
                for o in range(K):
                    for k in range(K):
                        w = [WB[:, qt % 2, h, k, j, o * P:(o + 1) * P] for h in range(2)]
                        mm = three((pO, pA)[n % 2][:, o, b * T:(b + 1) * T], w[0], w[1], XS[:, bb, 0, k, :],
                                   XS[:, bb, 1, k, :], k == 0, k == K - 1)
                if b == TB - 1:
                    mm.then_inc(o2_mm, 1)

            for qt in range(NQ + 1):
                if qt == 1:
                    pe.wait_ge(xs_ready, 3 * NT)
                for j in range(OG):
                    if qt < NQ:
                        mix(qt, j)
                    if qt:
                        apply(qt - 1, j)

            def expert3(e, par):
                wait_alone(pe, w_ready, e * N3P + N3_0 + N3P)
                gu = [lambda h, k, c, m=m: W3[:, par, m, h, k * H3 + c * P:k * H3 + (c + 1) * P] for m in (1, 0)]
                dn = lambda h, c, o: W3[:, par, 2, h, c * D + o * P:c * D + (o + 1) * P]
                groups(L3s, ST3, e, gu[0], gu[1], dn, HC3 // 2, ORDER3)

            pe.wait_ge(o2_ev, NT)
            with pe.Fori(0, E // 2, 1) as ep:
                for par in (0, 1):
                    expert3(pe.snap(ep * 2 + par), par)

        @block.scalar
        def _(act):
            def split_hi(t):
                nc.scalar.activation(XS[:, ds(t * TB, TB), 0, :, :].rearrange("p b k t -> p b (k t)"),
                                     XRd[:, ds(t * TB, TB), :], ACT.Copy, scale=XSC).then_inc(xs_hi, 1)

            act.wait_ge(r_exp, 1)
            nc.scalar.activation(EX, DD, ACT.Exp).then_inc(r_ex, 1)

            for t in range(NT):
                act.wait_ge(x_in[t], 16)
                split_hi(t)
            act.wait_ge(small_in, 16 * SMALL)
            with act.Fori(0, NT, 1) as t:
                act.wait_ge(h0_f, t + 1)
                nc.scalar.copy(HS[:, 0, 0:TN], HF[:, 0, :]).then_inc(h0_hi, 1)
                act.wait_ge(o0_mm, t + 1)
                act.wait_ge(o0_add, t + 1)
                for o in range(K):
                    i = nc.scalar.activation(GL[:, o, :], pO[:, o, :], ACT.Identity, bias=BI[:, o:o + 1], scale=INV)
                i.then_inc(o0_free, 1)
                act.wait_ge(o0_add, t + 2)
                split_hi(t)

            def hi(q, i, p, kc):
                act.wait_ge(q["gu_free"], i * kc + p + 3)
                act.wait_ge(q["h_free"], i * kc + p + 1)
                nc.scalar.activation(HSv[:, 0, 2 * p:2 * p + 2, :].rearrange("p c n -> p (c n)"),
                                     HF[:, p % 2, :], ACT.Copy, scale=XSC * INV).then_inc(q["h_hi"], 1)

            act.wait_ge(r_out, 2)
            n1 = act.value_load(ST1[0:1, E + 1:E + 2], min_val=1, max_val=G1)
            with act.Fori(0, n1, 1) as i:
                kc = IC1 // 2
                for p in range(kc):
                    act.wait_ge(L1s["gate_mm"], i * kc + p + 1)
                    act.wait_ge(L1s["gu_free"], i * kc + p + 1)
                    nc.scalar.activation(GL[:, p % 2, :], pG[:, p % 2, :], ACT.Gelu_apprx_tanh,
                                         scale=INV).then_inc(L1s["act_done"], 1)
                    hi(L1s, i, p, kc)

            def mixed_hi(qt, og):
                n = qt * OG + og
                if qt >= 2 and og == 0:
                    act.wait_ge(o2_mm, (qt - 1) * (QB // TB))
                act.wait_ge(b_mm, n + 1)
                nc.scalar.activation(
                    WB[:, qt % 2, 0, :, :, og * R:(og + 1) * R],
                    (pG, pU)[n // 2 % 2][:, n % 2, :].rearrange("p (k b o) -> p k b o", k=K, b=QB),
                    ACT.Copy, scale=1.0 / WSC).then_inc(b_hi, 1)

            def evacuate2(n):
                act.wait_ge(o2_mm, n + 1)
                act.wait_ge(o2_add, n) if n else None
                for o in range(K):
                    i2 = nc.scalar.activation(GL[:, o, :], (pO, pA)[n % 2][:, o, :], ACT.Identity,
                                              bias=BI[:, K + o:K + o + 1], scale=INV)
                i2.then_inc(o2_ev, 1)

            def split3_hi(n):
                act.wait_ge(o2_add, n + 1)
                split_hi(n)

            for j in range(OG // 2):
                mixed_hi(0, j)
            act.wait_ge(L1s["added"], n1 * GB + 1)
            for t in range(NT):
                split_hi(t)
                mixed_hi(0, OG // 2 + t)
            for qt in range(1, NQ + 1):
                for j in range(OG):
                    if qt < NQ:
                        mixed_hi(qt, j)
                    if j == TB + 1:
                        evacuate2((qt - 1) * 2)
                    if j == TB + 3:
                        split3_hi((qt - 1) * 2)
                    if j == 1 and qt > 1:
                        evacuate2(qt * 2 - 3)
                    if j == 3 and qt > 1:
                        split3_hi(qt * 2 - 3)
            evacuate2(NT - 1)
            split3_hi(NT - 1)

            with act.Fori(0, E, 1) as e:
                with group_loop(act, ST3, e) as i:
                    kc = HC3 // 2
                    for p in range(kc):
                        act.wait_ge(L3s["up_mm"], i * kc + p + 1)
                        act.wait_ge(L3s["gu_free"], i * kc + p + 1)
                        for c in (0, 1):
                            s = nc.scalar.activation(
                                GL[:, p % 2, c * GN:(c + 1) * GN], pU[:, p % 2, c * GN:(c + 1) * GN], ACT.Silu,
                                bias=BU[:, ds(e, 1), 2 * p + c], scale=INV)
                        s.then_inc(L3s["act_done"], 1)
                        hi(L3s, i, p, kc)
                    act.wait_ge(L3s["h_free"], (i + 2) * kc)
                    act.wait_ge(L3s["added"], i * GB + 1)
                    for o in range(K):
                        s = nc.scalar.activation(OV[:, o, :], pO[:, o, 0:GN], ACT.Identity,
                                                 bias=BD[:, ds(e, 1), o], scale=INV)
                    s.then_inc(L3s["o_free"], 1)

        @block.vector
        def _(dve):
            chain = [0]

            def step(ins):
                chain[0] += 1
                ins.then_inc(dve_step, 1)
                dve.wait_ge(dve_step, chain[0])

            def split_lo(t, n):
                dve.wait_ge(xs_hi, n)
                nc.vector.scalar_tensor_tensor(
                    out=XS[:, ds(t * TB, TB), 1, :, :].rearrange("p b k t -> p b (k t)"), in0=XRd[:, ds(t * TB, TB), :],
                    scalar=XSC, in1=XS[:, ds(t * TB, TB), 0, :, :].rearrange("p b k t -> p b (k t)"),
                    op0=ALU.mult, op1=ALU.subtract).then_inc(xs_ready, 1)

            for q, kc in ((L1s, IC1 // 2), (L3s, HC3 // 2)):
                nc.vector.nop().then_inc(q["gu_free"], 2)
                nc.vector.nop().then_inc(q["xg_free"], 2)
                nc.vector.nop().then_inc(q["h_free"], kc)
                nc.vector.nop().then_inc(q["added"], 1)
            nc.vector.nop().then_inc(L3s["o_free"], 1)
            nc.vector.nop().then_inc(o0_free, 1)
            nc.vector.nop().then_inc(o0_add, 1)

            dve.wait_ge(cond_in, 16)
            dve.wait_ge(consts, CONSTS)
            step(nc.vector.max(SO, LG))
            step(nc.vector.max_index(MI.bitcast(U32), SO, LG))
            step(nc.vector.tensor_copy(MIF, MI.bitcast(U32)))
            step(nc.vector.tensor_scalar(M1, IO[:, 0:E], MIF[:, 0:1], None, ALU.is_equal))
            step(nc.vector.tensor_scalar(M2, IO[:, 0:E], MIF[:, 1:2], None, ALU.is_equal))
            nc.vector.tensor_scalar(DD, SO, SO[:, 0:1], None, ALU.subtract).then_inc(r_exp, 1)
            dve.wait_ge(r_ex, 1)
            step(nc.vector.reduce_sum(SM[:, 0:1], EX, AX))
            step(nc.vector.reciprocal(SM[:, 1:2], SM[:, 0:1]))
            step(nc.vector.tensor_scalar(SM[:, 2:4], EX[:, 0:2], SM[:, 1:2], None, ALU.mult))
            step(nc.vector.reduce_sum(SM[:, 4:5], SM[:, 2:4], AX))
            step(nc.vector.reciprocal(SM[:, 5:6], SM[:, 4:5]))
            step(nc.vector.tensor_scalar(SM[:, 6:8], SM[:, 2:4], SM[:, 5:6], None, ALU.mult))
            step(nc.vector.tensor_scalar(SM[:, 2:4], SM[:, 6:8], 1.0 - TOP_SCALE, None, ALU.mult))
            step(nc.vector.scalar_tensor_tensor(out=SM[:, 0:2], in0=SM[:, 6:8], scalar=TOP_SCALE, in1=SM[:, 2:4],
                                                op0=ALU.mult, op1=ALU.add))
            step(nc.vector.tensor_scalar(WD[:, 0:E], M1, SM[:, 0:1], None, ALU.mult))
            step(nc.vector.scalar_tensor_tensor(out=WD[:, 0:E], in0=M2, scalar=SM[:, 1:2], in1=WD[:, 0:E],
                                                op0=ALU.mult, op1=ALU.add))
            step(nc.vector.memset(WD[:, E:], 1.0))
            step(nc.vector.tensor_tensor(MM[:, 0:E], M1, M2, ALU.add))
            step(nc.vector.memset(MM[:, E:], 1.0))
            nc.vector.tensor_scalar(CI.bitcast(I32), MM, 0.0, None, ALU.mult).then_inc(r_exp, 1)

            for layer, (ne, ns, starts, slots) in enumerate(((E + 1, S1, ST1, SL1), (E, S3, ST3, SL3))):
                if layer == 1:
                    step(nc.vector.tensor_copy(MM[:, 0:E], M1))
                    nc.vector.tensor_copy(RK[:, 0:1], M1[:, 0:1]).then_inc(r_exp, 2)
                dve.wait_ge(r_mm, layer + 1)
                step(nc.vector.tensor_scalar(CI[:, 0:ne].bitcast(I32), pA[0:B, 1, 0:ne], GB - 1.0, None, ALU.add))
                step(nc.vector.tensor_single_scalar(CI[:, 0:ne].bitcast(I32), CI[:, 0:ne].bitcast(I32), GB_LOG,
                                                    ALU.arith_shift_right))
                step(nc.vector.tensor_copy(CN[:, 0:ne], CI[:, 0:ne].bitcast(I32)))
                step(nc.vector.tensor_scalar(CN[:, 0:ne], CN[:, 0:ne], 1.0, None, ALU.max))
                step(nc.vector.memset(SF[:, 0:1], 0.0))
                for e in range(ne):
                    step(nc.vector.tensor_tensor(SF[:, e + 1:e + 2], SF[:, e:e + 1], CN[:, e:e + 1], ALU.add))
                step(nc.vector.tensor_copy(starts[0:1, 0:ne + 1], SF[0:1, 0:ne + 1]))
                step(nc.vector.scalar_tensor_tensor(out=PO_[:, 0:ne], in0=SF[:, 0:ne], scalar=float(GB),
                                                    in1=pA[0:B, 0, 0:ne], op0=ALU.mult, op1=ALU.add))
                step(nc.vector.scalar_tensor_tensor(out=PO_[:, 0:ne], in0=PO_[:, 0:ne], scalar=1.0, in1=MM[:, 0:ne],
                                                    op0=ALU.add, op1=ALU.mult))
                step(nc.vector.tensor_scalar(PO_[:, 0:ne], PO_[:, 0:ne], -1.0, None, ALU.add))
                for e in range(ne):
                    n = layer * (E + 1) + e
                    q = e % 2
                    if n >= 2:
                        dve.wait_ge(r_eqd, n - 1)
                    nc.vector.tensor_scalar(EQ[:, q * S1:q * S1 + ns], IO[:, 0:ns], PO_[:, e:e + 1], None,
                                            ALU.is_equal)
                    nc.vector.tensor_scalar(EQW[:, q * S1:q * S1 + ns], IO[:, 0:ns], PO_[:, e:e + 1],
                                            WD[:, e:e + 1], ALU.is_equal, ALU.mult).then_inc(r_eq, 1)
                dve.wait_ge(r_eqd, layer * (E + 1) + ne)
                step(nc.vector.tensor_scalar(slots[:, :], pO[0:1, 0, 0:ns], float(B), None, ALU.add))
                if layer == 0:
                    step(nc.vector.tensor_scalar(WS[:, :], pO[:, 1, 0:ns], INV, None, ALU.mult))
                nc.vector.tensor_copy(SM[:, 0:1], SM[:, 1:2]).then_inc(r_out, 1)

            dve.wait_ge(small_in, 16 * SMALL)
            nc.vector.tensor_scalar(CW[:, :], YR[:, :], 2.0 * XSC * INV, None, ALU.mult).then_inc(tables, 1)
            nc.vector.tensor_scalar(BG[:, :, :], BG[:, :, :], 1.0 / INV, None, ALU.mult).then_inc(tables, 1)
            step(nc.vector.tensor_tensor(YF.rearrange("p (b o) -> p b o", b=B),
                                         YR[:, :].unsqueeze(2).to_broadcast([P, B, R]),
                                         DG[:, :].unsqueeze(1).to_broadcast([P, B, R]), ALU.mult))
            step(nc.vector.tensor_scalar(YF, YF, WSC, None, ALU.mult))
            step(nc.vector.tensor_copy(YB[:, 0, :], YF))
            nc.vector.tensor_tensor(YB[:, 1, :], YF, YB[:, 0, :], ALU.subtract).then_inc(tables, 1)
            dve.wait_ge(tables, TABLES)

            for t in range(NT):
                split_lo(t, t + 1)

            def tile0(t, par):
                dve.wait_ge(h0_mm, t + 1)
                nc.vector.tensor_tensor(HF[:, 0, :].rearrange("p (b t) -> p b t", b=TB),
                                        pA[:, par, :].rearrange("p (b t) -> p b t", b=TB),
                                        CW[:, ds(t * TB, TB)].unsqueeze(2).to_broadcast([P, TB, T]), ALU.mult).then_inc(h0_f, 1)
                dve.wait_ge(h0_hi, t + 1)
                nc.vector.tensor_tensor(HS[:, 1, 0:TN], HF[:, 0, :], HS[:, 0, 0:TN], ALU.subtract).then_inc(h0_ready, 1)
                dve.wait_ge(o0_free, t + 2)
                for o in range(K):
                    x = XR[:, ds(t * TB, TB), o, :]
                    i = nc.vector.tensor_tensor(x, GL[:, o, :].rearrange("p (b t) -> p b t", b=TB), x, ALU.add)
                i.then_inc(o0_add, 1)
                split_lo(t, t + (NT + 1))

            with dve.Fori(0, NT // 2, 1) as tp:
                for par in (0, 1):
                    tile0(dve.snap(tp * 2 + par), par)

            def hidden_lo(q, i, p, kc):
                dve.wait_ge(q["h_hi"], i * kc + p + 1)
                nc.vector.scalar_tensor_tensor(
                    out=HSv[:, 1, 2 * p:2 * p + 2, :].rearrange("p c n -> p (c n)"), in0=HF[:, p % 2, :],
                    scalar=XSC * INV, in1=HSv[:, 0, 2 * p:2 * p + 2, :].rearrange("p c n -> p (c n)"),
                    op0=ALU.mult, op1=ALU.subtract).then_inc(q["h_ready"], 1)

            n1 = dve.value_load(ST1[0:1, E + 1:E + 2], min_val=1, max_val=G1)
            with dve.Fori(0, n1, 1) as i:
                kc = IC1 // 2
                for p in range(kc):
                    dve.wait_ge(L1s["act_done"], i * kc + p + 1)
                    dve.wait_ge(L1s["up_mm"], i * kc + p + 1)
                    nc.vector.tensor_tensor(HF[:, p % 2, :], pU[:, p % 2, :], GL[:, p % 2, :],
                                            ALU.mult).then_inc(L1s["gu_free"], 1)
                    hidden_lo(L1s, i, p, kc)
                bs = [dve.value_load(SL1[0:1, ds(i * GB + s, 1)], min_val=0, max_val=B) for s in range(GB)]
                dve.wait_ge(L1s["h_free"], (i + 2) * (IC1 // 2))
                for s in range(GB):
                    x = XR[:, ds(bs[s], 1), :, :].rearrange("p b k t -> p (b k) t")
                    dve.wait_ge(L1s["added"], i * GB + s + 1)
                    ins = nc.vector.scalar_tensor_tensor(
                        out=x, in0=pO[:, :, s * T:(s + 1) * T], scalar=WS[:, ds(i * GB + s, 1)], in1=x,
                        op0=ALU.mult, op1=ALU.add)
                    ins.then_inc(L1s["added"], 1)

            def mixed_lo(qt, og):
                n = qt * OG + og
                dve.wait_ge(b_hi, n + 1)
                dst = [WB[:, qt % 2, h, :, :, og * R:(og + 1) * R].rearrange("p k b o -> p (k b) o") for h in (0, 1)]
                nc.vector.scalar_tensor_tensor(
                    out=dst[1], in0=(pG, pU)[n // 2 % 2][:, n % 2, :].rearrange("p (m o) -> p m o", o=R),
                    scalar=1.0 / WSC, in1=dst[0], op0=ALU.mult, op1=ALU.subtract).then_inc(b_ready, 1)

            def add2(n):
                dve.wait_ge(o2_ev, n + 1)
                for o in range(K):
                    x = XR[:, n * TB:(n + 1) * TB, o, :]
                    i2 = nc.vector.tensor_tensor(x, GL[:, o, :].rearrange("p (b t) -> p b t", b=TB), x, ALU.add)
                i2.then_inc(o2_add, 1)

            for j in range(OG // 2):
                mixed_lo(0, j)
            for t in range(NT):
                split_lo(t, t + (2 * NT + 1))
                mixed_lo(0, OG // 2 + t)
            for qt in range(1, NQ + 1):
                for j in range(OG):
                    if qt < NQ:
                        mixed_lo(qt, j)
                    if j == TB + 1:
                        add2((qt - 1) * 2)
                    if j == TB + 3:
                        split_lo((qt - 1) * 2, (qt - 1) * 2 + 3 * NT + 1)
                    if j == 1 and qt > 1:
                        add2(qt * 2 - 3)
                    if j == 3 and qt > 1:
                        split_lo(qt * 2 - 3, qt * 2 - 3 + 3 * NT + 1)
            add2(NT - 1)
            split_lo(NT - 1, 4 * NT)

            with dve.Fori(0, E, 1) as e:
                with group_loop(dve, ST3, e) as i:
                    kc = HC3 // 2
                    for p in range(kc):
                        dve.wait_ge(L3s["act_done"], i * kc + p + 1)
                        dve.wait_ge(L3s["gate_mm"], i * kc + p + 1)
                        for c in (0, 1):
                            m = slice(c * GN, (c + 1) * GN)
                            ins = nc.vector.scalar_tensor_tensor(
                                out=HF[:, p % 2, m], in0=pG[:, p % 2, m], scalar=BG[:, ds(e, 1), 2 * p + c],
                                in1=GL[:, p % 2, m], op0=ALU.add, op1=ALU.mult)
                        ins.then_inc(L3s["gu_free"], 1)
                        hidden_lo(L3s, i, p, kc)
                    bs = [dve.value_load(SL3[0:1, ds(i * GB + s, 1)], min_val=0, max_val=B) for s in range(GB)]
                    dve.wait_ge(L3s["o_free"], i + 2)
                    for s in range(GB):
                        x = XR[:, ds(bs[s], 1), :, :].rearrange("p b k t -> p (b k) t")
                        dve.wait_ge(L3s["added"], i * GB + s + 1)
                        ins = nc.vector.tensor_tensor(x, OV[:, :, s * T:(s + 1) * T], x, ALU.add)
                        ins.then_inc(L3s["added"], 1)


SHAPES = {"x": (P, B, K * T), "cond_8": (B, E), "condT": (E, B), "w0": (P, PIECE), "L0_cond_b_base": (P, K),
          "L1_cond_skill_gate": (E, D, I1), "L1_cond_skill_up": (E, D, I1), "L1_cond_skill_down": (E, I1, D),
          "L1_cond_shared_gate": (D, I1), "L1_cond_shared_up": (D, I1), "L1_cond_shared_down": (I1, D),
          "w2": (P, OG * D), "mask": (R, OG * D), "L2_cond_bias": (P, K),
          "L3_cond_W_up": (E, P, K * H3), "L3_cond_W_gate": (E, P, K * H3), "L3_cond_W_down": (E, P, HC3 * D),
          "L3_cond_b_up": (P, E, HC3), "L3_cond_b_gate": (P, E, HC3), "L3_cond_b_down": (P, E, K)}


def layouts(v, np):
    def chunks(w):
        *lead, m, c = w.shape
        w = w.reshape(*lead, m, c // P, P)
        n = len(lead)
        return w.transpose(*range(n), n + 2, n + 1, n).reshape(*lead, P, c // P * m)

    r = {"x": v["x"].reshape(B, T, K, P).transpose(3, 0, 2, 1),
         "cond_8": v["cond_8"], "condT": v["cond_8"].T,
         "w0": np.concatenate([chunks(v["L0_cond_W_base"]), chunks(v["L0_cond_As"].reshape(P, D)),
                               v["L0_cond_Bs"].transpose(0, 2, 1).reshape(P, D)], axis=1),
         "w2": v["L2_cond_weight"].reshape(E, OG, R, D).transpose(0, 2, 1, 3),
         "mask": v["L2_cond_mask"].reshape(OG, R, D).transpose(1, 0, 2),
         "L3_cond_W_up": chunks(v["L3_cond_W_up"]), "L3_cond_W_gate": chunks(v["L3_cond_W_gate"]),
         "L3_cond_W_down": chunks(v["L3_cond_W_down"])}
    for n in ("L0_cond_b_base", "L2_cond_bias"):
        r[n] = v[n].reshape(K, P).T
    for n in ("L3_cond_b_up", "L3_cond_b_gate", "L3_cond_b_down"):
        r[n] = v[n].reshape(E, -1, P).transpose(2, 0, 1)
    for n in SHAPES:
        r[n] = np.ascontiguousarray(r[n] if n in r else v[n]).reshape(SHAPES[n])
    return r


def kernel(**inputs):
    import numpy as np
    import concourse.bacc as bacc
    from concourse.bass_utils import run_bass_kernel_spmd

    nc = bacc.Bacc("TRN2", target_bir_lowering=False, num_devices=1)
    arrays = {f"in_{n}": v for n, v in layouts({n: np.asarray(v) for n, v in inputs.items()}, np).items()}
    aps = {n: nc.dram_tensor(f"in_{n}", SHAPES[n], F32, kind="ExternalInput").ap() for n in SHAPES}
    out = nc.dram_tensor("out_0", (P, B, K * T), F32, kind="ExternalOutput").ap()
    build(nc, aps, out)
    r = run_bass_kernel_spmd(nc, [arrays], core_ids=[0])
    got = r.results[0]["out_0"]
    return np.ascontiguousarray(got.reshape(P, B, K, T).transpose(1, 3, 2, 0)).reshape(B, T, D)
```
